# Optimizing a Trainium2 kernel written in Bass

```python
import numpy as np
import jax
import jax.numpy as jnp

def _softmax(x, axis=-1):
    return jax.nn.softmax(x, axis=axis)

def _gelu(x):
    return jax.nn.gelu(x, approximate=True)

def _silu(x):
    return jax.nn.silu(x)

def _sigmoid(x):
    return jax.nn.sigmoid(x)

def _layernorm(x, axis=-1, eps=1e-05):
    m = jnp.mean(x, axis=axis, keepdims=True)
    v = jnp.var(x, axis=axis, keepdims=True)
    return (x - m) / jnp.sqrt(v + eps)

def _scatter_add(tgt, idx, src, axis=0):
    return tgt.at[idx].add(src)

def _segment_sum(src, seg, n):
    return jax.ops.segment_sum(src, seg, n)
kernel_name = 'mk_macaron_d1_jaxref_r8_7987ab'

def setup_inputs(seed: int=0):
    np.random.seed(seed)
    _w = jnp.asarray

    def _L0_attn_setup():
        import jax, jax.numpy as jnp
        import numpy as np
        B, T, C = (4, 512, 256)

        def _scan_op(a, bb):
            g_i, v_i = a
            g_j, v_j = bb
            return (g_j * g_i, g_j * v_i + v_j)
        key = jax.random.key(seed)
        k1, k2 = jax.random.split(key)
        x = jax.random.normal(k1, (B, T, C), dtype=jnp.float32)
        W = jax.random.normal(k2, (2 * C, C), dtype=jnp.float32) * (1.0 / np.sqrt(C))
        b = jnp.zeros((2 * C,), dtype=jnp.float32)
        return {'x': x, 'W': W, 'b': b}
    _L0_attn_in = _L0_attn_setup()

    def _L0_ffn_setup():
        import jax, jax.numpy as jnp
        import numpy as np
        TOP_K = 6
        CAP_FACTOR = 2

        def _shared_swiglu(x, wg, wu, wd):
            return jax.nn.silu(x @ wg.T) * (x @ wu.T) @ wd.T
        key = jax.random.key(seed)
        ks = jax.random.split(key, 8)
        B, S, D, E, F, FS = (4, 256, 256, 64, 176, 352)
        scale = jnp.float32(0.02)
        return {'hidden_states': jax.random.normal(ks[0], (B, S, D), jnp.float32), 'gate_w': jax.random.normal(ks[1], (E, D), jnp.float32) * scale, 'w_gate': jax.random.normal(ks[2], (E, F, D), jnp.float32) * scale, 'w_up': jax.random.normal(ks[3], (E, F, D), jnp.float32) * scale, 'w_down': jax.random.normal(ks[4], (E, D, F), jnp.float32) * scale, 'sh_gate': jax.random.normal(ks[5], (FS, D), jnp.float32) * scale, 'sh_up': jax.random.normal(ks[6], (FS, D), jnp.float32) * scale, 'sh_down': jax.random.normal(ks[7], (D, FS), jnp.float32) * scale}
    _L0_ffn_in = _L0_ffn_setup()
    _d = {'L0_attn_x': _L0_attn_in['x'], 'L0_attn_W': _L0_attn_in['W'], 'L0_attn_b': _L0_attn_in['b'], 'L0_ffn_gate_w': _L0_ffn_in['gate_w'], 'L0_ffn_w_gate': _L0_ffn_in['w_gate'], 'L0_ffn_w_up': _L0_ffn_in['w_up'], 'L0_ffn_w_down': _L0_ffn_in['w_down'], 'L0_ffn_sh_gate': _L0_ffn_in['sh_gate'], 'L0_ffn_sh_up': _L0_ffn_in['sh_up'], 'L0_ffn_sh_down': _L0_ffn_in['sh_down']}
    _x0 = _d['L0_attn_x']
    _d['L0_attn_x'] = jax.random.normal(jax.random.fold_in(jax.random.key(seed), 1), (2, 2048, 256), dtype=_x0.dtype)
    del _x0
    return _d

def reference(L0_attn_x, L0_attn_W, L0_attn_b, L0_ffn_gate_w, L0_ffn_w_gate, L0_ffn_w_up, L0_ffn_w_down, L0_ffn_sh_gate, L0_ffn_sh_up, L0_ffn_sh_down):

    def _L0_attn_ref(x, W, b):
        import jax, jax.numpy as jnp
        import numpy as np
        B, T, C = (4, 512, 256)

        def _scan_op(a, bb):
            g_i, v_i = a
            g_j, v_j = bb
            return (g_j * g_i, g_j * v_i + v_j)
        params = jnp.einsum('btc,dc->btd', x, W) + b
        gates, values = jnp.split(params, 2, axis=-1)
        gates = jax.nn.sigmoid(gates)
        values = jnp.tanh(values)
        _, hidden = jax.lax.associative_scan(_scan_op, (gates, values), axis=1)
        return hidden

    def _L0_ffn_ref(hidden_states, gate_w, w_gate, w_up, w_down, sh_gate, sh_up, sh_down):
        import jax, jax.numpy as jnp
        import numpy as np
        TOP_K = 6
        CAP_FACTOR = 2

        def _shared_swiglu(x, wg, wu, wd):
            return jax.nn.silu(x @ wg.T) * (x @ wu.T) @ wd.T
        B, S, D = hidden_states.shape
        E = gate_w.shape[0]
        x = hidden_states.reshape(-1, D)
        N = x.shape[0]
        A = N * TOP_K
        C = CAP_FACTOR * ((A + E - 1) // E)
        scores = jax.nn.softmax(x @ gate_w.T, axis=-1)
        topk_w, topk_idx = jax.lax.top_k(scores, TOP_K)
        topk_w = topk_w / (topk_w.sum(-1, keepdims=True) + 1e-20)
        flat_e = topk_idx.reshape(-1)
        flat_w = topk_w.reshape(-1)
        order = jnp.argsort(flat_e)
        se = flat_e[order]
        st = order // TOP_K
        sw = flat_w[order]
        counts = jnp.bincount(flat_e, length=E)
        offsets = jnp.cumsum(counts) - counts
        pos = jnp.arange(A) - offsets[se]
        valid = pos < C
        pos_c = jnp.minimum(pos, C - 1)
        buf = jnp.zeros((E, C, D), x.dtype).at[se, pos_c].add(jnp.where(valid[:, None], x[st], jnp.zeros((), x.dtype)))
        g = jnp.einsum('ecd,efd->ecf', buf, w_gate)
        u = jnp.einsum('ecd,efd->ecf', buf, w_up)
        eo = jnp.einsum('ecf,edf->ecd', jax.nn.silu(g) * u, w_down)
        gathered = eo[se, pos_c] * (sw * valid.astype(sw.dtype))[:, None]
        y = jnp.zeros_like(x).at[st].add(gathered).reshape(B, S, D)
        return y + _shared_swiglu(hidden_states, sh_gate, sh_up, sh_down)
    x = L0_attn_x
    x = x + 0.5 * _L0_ffn_ref(_layernorm(x, axis=-1), L0_ffn_gate_w, L0_ffn_w_gate, L0_ffn_w_up, L0_ffn_w_down, L0_ffn_sh_gate, L0_ffn_sh_up, L0_ffn_sh_down)
    x = x + _L0_attn_ref(_layernorm(x, axis=-1), L0_attn_W, L0_attn_b)
    x = x + 0.5 * _L0_ffn_ref(_layernorm(x, axis=-1), L0_ffn_gate_w, L0_ffn_w_gate, L0_ffn_w_up, L0_ffn_w_down, L0_ffn_sh_gate, L0_ffn_sh_up, L0_ffn_sh_down)
    return x

_drawn_inputs = setup_inputs


def setup_inputs(seed=0):
    import zlib

    import numpy as np

    out = dict(_drawn_inputs(seed))
    spreads = {'L0_attn_b': (0.0, 0.1)}
    factors = {'L0_ffn_gate_w': 8.0,
     'L0_ffn_w_gate': 8.0,
     'L0_ffn_w_up': 8.0,
     'L0_ffn_w_down': 8.0,
     'L0_ffn_sh_gate': 3.638,
     'L0_ffn_sh_up': 3.606,
     'L0_ffn_sh_down': 3.593}
    for name, (base, spread) in spreads.items():
        noise = np.random.default_rng([zlib.crc32(name.encode()), seed]).standard_normal(out[name].shape)
        drawn = base * np.exp(spread * noise) if base else spread * noise
        out[name] = jnp.asarray(drawn.astype(out[name].dtype))
    for name, factor in factors.items():
        out[name] = (out[name] * factor).astype(out[name].dtype)
    return out
```

```python
from contextlib import ExitStack

import concourse.bass as bass
from concourse import mybir

F32 = mybir.dt.float32
F16 = mybir.dt.float16
I32 = mybir.dt.int32
U32 = mybir.dt.uint32
ALU = mybir.AluOpType
ACT = mybir.ActivationFunctionType
X = mybir.AxisListType.X
P = 128


class Steps:

    def __init__(self, eng, sem):
        self.eng, self.sem, self.n, self.offset, self.start = eng, sem, 0, 0, 0

    def mark(self, instruction):
        instruction.then_inc(self.sem, 1)
        self.n += 1

    def mark_none(self):
        self.eng.sem_inc(self.sem, 1)
        self.n += 1

    def sync(self):
        self.eng.wait_ge(self.sem, self.offset + self.n)

    def enter(self, i, per):
        self.start, self.per, self.offset = self.n, per, i * per

    def leave(self, count):
        assert self.n - self.start == self.per, self.n - self.start
        self.n, self.offset = self.start + self.per * count, 0


def macaron(nc, x_in, w_attn, b_attn, gate_w, w_gu, w_dn, sh_gate, sh_up, sh_down, out, TOPK, CAP):
    N, D = x_in.shape
    DC = D // P
    NT = N // P
    G = 4
    NG = NT // G
    T = G * P
    E = gate_w.shape[2]
    F = w_gu.shape[2] // (2 * DC)
    FH = F // 2
    FS = sh_gate.shape[2]
    FW = [min(118, FS - f) for f in range(0, FS, 118)]
    FO = [0, 118, 236]
    WG, WD = DC * 2 * F, 2 * D
    WR = 4
    NB = 256
    assert NB >= N * TOPK // P + E - 1
    AHEAD = 4
    NBP = NB + AHEAD
    U = 8
    DROPPED = 32768.0
    HB = N // 2
    CH = 2 * D

    xn_dram = nc.dram_tensor("xn_rows", (N, D), F32).ap()
    y_dram = nc.dram_tensor("y_rows", (N * TOPK, D), F32).ap()

    ctx = ExitStack()
    with ctx:
        def sb(name, shape, dt=F32):
            return ctx.enter_context(nc.sbuf_tensor(name, shape, dt))

        def sem(name):
            return ctx.enter_context(nc.semaphore(name))

        def sems(name, n):
            return [sem(f"{name}{i}") for i in range(n)]

        bank = [ctx.enter_context(nc.psum_tensor(f"bank{i}", [P, 512], F32)) for i in range(8)]

        ident = sb("ident", [P, P])
        before = sb("before", [P, P], F16)
        upto = sb("upto", [P, P], F16)
        ones = sb("ones", [P, P], F16)
        none = sb("none", [P, P], F16)
        iota = sb("iota", [P, NB], F16)
        tokval = sb("tokval", [P, NT])
        eps = sb("eps", [P, 1])
        gw = sb("gw", [P, DC, E])
        shg = sb("shg", [P, DC, FS])
        shu = sb("shu", [P, DC, FS])
        shd = sb("shd", [P, len(FW), D])
        wat = sb("wat", [P, DC, CH])
        bat = sb("bat", [P, CH // P])
        xs = sb("xs", [P, NT, D])
        st = sb("st", [P, U, 6])
        mv8 = sb("mv8", [P, U, 2])
        mv = sb("mv", [P, NT, 2])
        sd = sb("sd", [P, NT])
        rs = sb("rs", [P, NT])
        xnb = sb("xnb", [P, G, D])
        xt = sb("xt", [P, 2, DC, T])
        lg = sb("lg", [P, G, E])
        ex = sb("ex", [P, G, E])
        pr = sb("pr", [P, G, E])
        g4 = sb("g4", [P, 4, G])
        top8 = sb("top8", [P, G, 8])
        idx8 = sb("idx8", [P, G, 8], U32)
        idxf = sb("idxf", [P, G, 8], F16)
        msum = sb("msum", [P, E], F16)
        onehot = sb("onehot", [P, NT, TOPK, E], F16)
        mask = sb("mask", [P, 2, G, E], F16)
        carry = sb("carry", [P, 2, E], F16)
        topp = sb("topp", [P, NT, 8])
        pos = sb("pos", [P, NT, E])
        sg = sb("sg", [P, 2, T])
        hs = sb("hs", [P, len(FW), T])
        col = sb("col", [P, 8])
        coli = sb("coli", [P, 2], I32)
        nbf = sb("nbf", [E, 1], F16)
        nbb = sb("nbb", [E, P], F16)
        ge = sb("ge", [E, NB], F16)
        start = sb("start", [P, E])
        erow = sb("erow", [1, NBP], I32)
        endrow = sb("endrow", [1, WR + E], I32)
        v1 = sb("v1", [P, G, E])
        v2 = sb("v2", [P, G, E])
        v3 = sb("v3", [P, G, E])
        pick = sb("pick", [P, G, TOPK, E])
        slot = sb("slot", [P, NT * TOPK])
        sloti = sb("sloti", [P, NT * TOPK], I32)
        blki = sb("blki", [P, NT * TOPK], I32)
        blk = sb("blk", [P, NT * TOPK])
        low = sb("low", [P, NT * TOPK])
        cur = sb("cur", [P, 2, 2, 8])
        wsum = sb("wsum", [P, NT])
        wrec = sb("wrec", [P, NT])
        wc = sb("wc", [P, NT, TOPK])
        wv = sb("wv", [P, NT, TOPK])
        oblk = sb("oblk", [P, 2, TOPK, NB], F16)
        otok = sb("otok", [P, 2, TOPK, P], F16)
        orow = sb("orow", [P, 2, TOPK, P], F16)
        tok = sb("tok", [P, NBP], U32)
        row = sb("row", [P, NB], U32)
        f1 = sb("f1", [P, NB])
        f2 = sb("f2", [P, NB])
        wring = sb("wring", [P, WR, WG + WD])
        gidx = sb("gidx", [P, 2, AHEAD], U32)
        ridx = sb("ridx", [P, 2, AHEAD], U32)
        xg = sb("xg", [P, U, D])
        xgt = sb("xgt", [P, 2, DC, P])
        sge = sb("sge", [P, 2, F])
        he = sb("he", [P, 2, F])
        het = sb("het", [P, 2, 2, P])
        eo = sb("eo", [P, 4, D])
        yb = sb("yb", [P, G, TOPK * D])
        spare = onehot[:, :, :, :].rearrange("p t k e -> p (t k e)").bitcast(F32)
        gates = spare[:, 0:2 * T].rearrange("p (c t) -> p c t", c=2)
        values = spare[:, 2 * T:4 * T].rearrange("p (c t) -> p c t", c=2)
        hid = spare[:, 4 * T:8 * T].rearrange("p (b c t) -> p b c t", b=2, c=2)

        made = sem("made")
        made2 = sem("made2")
        x_in_s = sems("x_in", 4)
        w_in = sem("w_in")
        y_zero = sem("y_zero")
        dve_step = sem("dve_step")
        act_step = sem("act_step")
        stats = sem("stats")
        sd_ready = sem("sd_ready")
        rs_ready = sem("rs_ready")
        xn_ready = sem("xn_ready")
        xn_stored = sems("xn_stored", G)
        tx_done = sem("tx_done")
        xt_free = sem("xt_free")
        lg_done = sem("lg_done")
        lg_read = sem("lg_read")
        exp_done = sem("exp_done")
        mask_ready = sem("mask_ready")
        carry_ready = sem("carry_ready")
        pos_done = sem("pos_done")
        pos_saved = sem("pos_saved")
        gu_done = sem("gu_done")
        sg_ready = sem("sg_ready")
        h_free = sem("h_free")
        dn_done = sem("dn_done")
        xs_added = sem("xs_added")
        cnt_done = sem("cnt_done")
        nb_ready = sem("nb_ready")
        start_done = sem("start_done")
        ge_ready = sem("ge_ready")
        e_done = sem("e_done")
        plan_ready = sem("plan_ready")
        oh_ready = sem("oh_ready")
        oh_used = sem("oh_used")
        list_done = sem("list_done")
        list_ready = sem("list_ready")
        pool_step = sem("pool_step")
        xg_in = sems("xg_in", U)
        xgt_done = sem("xgt_done")
        xgt_ready = sem("xgt_ready")
        egu_done = sem("egu_done")
        esg_ready = sem("esg_ready")
        eh_ready = sem("eh_ready")
        eht_done = sem("eht_done")
        eht_ready = sem("eht_ready")
        edn_done = sem("edn_done")
        eo_ready = sem("eo_ready")
        eo_out = sems("eo_out", 4)
        w_load = sems("w_load", WR)
        w_ready = sem("w_ready")
        y_in = sems("y_in", G)
        comb = sem("comb")
        at_done = sem("at_done")
        at_act = sem("at_act")
        hid_ready = sem("hid_ready")
        ht_done = sem("ht_done")
        at_x = sem("at_x")
        stored = sem("stored")

        block = ctx.enter_context(nc.Block())

        psT = [bank[s][:, 0:D] for s in range(2)]
        LG = bank[7][:, 0:G * E].rearrange("p (t e) -> p t e", t=G)
        PO = bank[7][:, G * E:2 * G * E].rearrange("p (t e) -> p t e", t=G)

        def tiles_before(phase):
            return {"moe0": 0, "attn": NT, "moe1": 2 * NT}[phase]

        @block.sync
        def _(sp):
            xv = x_in.rearrange("(t p) d -> p t d", p=P)
            for q in range(4):
                sp.dma_start(xs[:, q * 8:(q + 1) * 8, :], xv[:, q * 8:(q + 1) * 8, :]).then_inc(x_in_s[q], 16)
            sp.dma_start(gw[:, :, :], gate_w).then_inc(w_in, 16)
            sp.dma_start(shg[:, :, :], sh_gate).then_inc(w_in, 16)
            sp.dma_start(shu[:, :, :], sh_up).then_inc(w_in, 16)
            for c, w in enumerate(FW):
                sp.dma_start(shd[0:w, c, :], sh_down[FO[c]:FO[c] + w, :]).then_inc(w_in, 16)
            sp.dma_start(wat[:, :, :], w_attn).then_inc(w_in, 16)
            sp.dma_start(bat[:, :], b_attn).then_inc(w_in, 16)
            sp.wait_ge(made2, 1)
            yz = y_dram.rearrange("(t p k) d -> t p (k d)", p=P, k=TOPK)
            with sp.Fori(0, NT) as t:
                sp.dma_start(yz[bass.ds(t, 1), :, :].rearrange("a p m -> (a p) m"), yb[:, 0, :]).then_inc(y_zero, 16)

            def moe(L):
                nb = NB * L
                with sp.Fori(0, NG) as g:
                    for u in range(G):
                        sp.wait_ge(xn_ready, tiles_before(f"moe{L}") + g * G + u + 1)
                        sp.dma_start(xn_dram[bass.ds((g * G + u) * P, P), :], xnb[:, u, :]).then_inc(xn_stored[u], 16)
                sp.wait_ge(plan_ready, L + 1)
                with sp.Fori(0, E // WR) as q:
                    for u in range(WR):
                        end = sp.value_load(endrow[0:1, bass.ds(q * WR + u, 1)], min_val=0, max_val=NB)
                        sp.wait_ge(edn_done, end + nb)
                        sp.dma_start(wring[:, u, 0:WG], w_gu[bass.ds(q * WR + u, 1), :, :].rearrange("a p m -> (a p) m")).then_inc(w_load[u], 16)
                        sp.dma_start(wring[0:FH, u, WG:WG + WD], w_dn[bass.ds(q * WR + u, 1), :, :].rearrange("a p m -> (a p) m")).then_inc(w_load[u], 16)
                        sp.wait_ge(w_load[u], 32 * (q + 1) + 32 * (E // WR) * L)
                        sp.sem_inc(w_ready, 1)
                for j in range(AHEAD):
                    sp.wait_ge(xg_in[j], 16 * (NB // U + 1) * (L + 1))
                for s in range(4):
                    sp.wait_ge(eo_out[s], 16 * (NB // 4) * (L + 1))
                with sp.Fori(0, NG) as g:
                    for u in range(G):
                        sp.wait_ge(comb, NG * L + g)
                        sp.dma_start(yb[:, u, :], yz[bass.ds(g * G + u, 1), :, :].rearrange("a p m -> (a p) m")).then_inc(y_in[u], 16)

            moe(0)
            moe(1)
            ov = out.rearrange("(t p) d -> p t d", p=P)
            for q in range(NG):
                sp.wait_ge(comb, NG + q + 1)
                sp.dma_start(ov[:, q * G:(q + 1) * G, :], xs[:, q * G:(q + 1) * G, :]).then_inc(stored, 16)
            sp.wait_ge(stored, 16 * NG)

        @block.gpsimd
        def _(pool):
            pool.memset(ident[:, :], 0.0).then_inc(made, 1)
            pool.memset(before[:, :], 1.0).then_inc(made, 1)
            pool.memset(upto[:, :], 1.0).then_inc(made, 1)
            pool.memset(yb[:, 0, :], 0.0).then_inc(made2, 1)
            pool.memset(ones[:, :], 1.0).then_inc(made, 1)
            pool.memset(none[:, :], 0.0).then_inc(made, 1)
            pool.memset(eps[:, :], 1e-5).then_inc(made, 1)
            pool.memset(tok[:, NB:NBP], 2048).then_inc(made, 1)
            pool.memset(erow[:, NB:NBP], E - 1).then_inc(made, 1)
            pool.memset(endrow[:, 0:WR], 0).then_inc(made, 1)
            pool.iota(iota[:, :], pattern=[[1, NB]], base=0, channel_multiplier=0,
                      allow_small_or_imprecise_dtypes=True).then_inc(made, 1)
            pool.iota(tokval[:, :], pattern=[[P, NT]], base=-2048, channel_multiplier=1,
                      allow_small_or_imprecise_dtypes=True).then_inc(made, 1)
            pool.wait_ge(made, 11)
            pool.affine_select(out=ident[:, :], in_=ident[:, :], compare_op=ALU.not_equal, fill=1.0,
                               base=0, pattern=[[-1, P]], channel_multiplier=1).then_inc(made, 1)
            pool.affine_select(out=before[:, :], in_=before[:, :], compare_op=ALU.is_gt, fill=0.0,
                               base=0, pattern=[[1, P]], channel_multiplier=-1).then_inc(made, 1)
            pool.affine_select(out=upto[:, :], in_=upto[:, :], compare_op=ALU.is_ge, fill=0.0,
                               base=0, pattern=[[1, P]], channel_multiplier=-1).then_inc(made, 1)
            step = Steps(pool, pool_step)

            def gather(slot8, index):
                pool.indirect_dma_start(out=xg[:, slot8, :], out_offset=None, in_=xn_dram,
                                        in_offset=bass.IndirectOffsetOnAxis(ap=index, axis=0)).then_inc(xg_in[slot8], 16)

            def moe(L):
                pool.wait_ge(list_ready, L + 1)
                for u in range(G):
                    pool.wait_ge(xn_stored[u], 16 * NG * (L + 1))
                step.mark(pool.tensor_copy(gidx[:, 0, :], tok[:, 0:AHEAD]))
                step.sync()
                for j in range(AHEAD):
                    gather(j, gidx[:, 0, j:j + 1])
                if L == 0:
                    pool.wait_ge(y_zero, 16 * NT)
                with pool.Fori(0, NB // U) as it:
                    step.enter(it, 3 * (U // AHEAD) + U)
                    for u in range(U):
                        h = u // AHEAD
                        if u % AHEAD == 0:
                            step.mark(pool.tensor_copy(gidx[:, 1 - h, :], tok[:, bass.ds(it * U + u + AHEAD, AHEAD)]))
                            step.mark(pool.tensor_copy(ridx[:, h, :], row[:, bass.ds(it * U + u, AHEAD)]))
                            step.sync()
                            step.mark_none()
                        gather((u + AHEAD) % U, gidx[:, 1 - h, u % AHEAD:u % AHEAD + 1])
                        pool.wait_ge(eo_ready, it * U + u + 3 + NB * L)
                        step.mark_none()
                        pool.indirect_dma_start(out=y_dram, out_offset=bass.IndirectOffsetOnAxis(ap=ridx[:, h, u % AHEAD:u % AHEAD + 1], axis=0),
                                                in_=eo[:, u % 4, :], in_offset=None,
                                                bounds_check=N * TOPK - 1, oob_is_err=False).then_inc(eo_out[u % 4], 16)
                step.leave(NB // U)
                for j in range(AHEAD):
                    pool.wait_ge(xg_in[j], 16 * ((NB // U + 1) * (L + 1)))

            moe(0)
            moe(1)

        @block.scalar
        def _(act):
            act.wait_ge(made, 14)
            act.sem_inc(xt_free, 2)
            step = Steps(act, act_step)

            def copy_tiles(first, gb, g):
                for u in range(G):
                    act.wait_ge(tx_done, first + g * G + u + 1)
                    act.activation(xt[:, gb, :, u * P:(u + 1) * P], psT[u % 2].rearrange("p (c t) -> p c t", c=DC),
                                   ACT.Copy).then_inc(xt_free, 1)

            def moe(L):
                act.wait_ge(stats, 2 * L + 1)
                act.activation(sd[:, :], mv[:, :, 1], ACT.Sqrt, bias=eps[:, 0:1]).then_inc(sd_ready, 1)
                with act.Fori(0, NG // 2) as it:
                    for gb in range(2):
                        g = it * 2 + gb
                        copy_tiles(tiles_before(f"moe{L}"), gb, g)
                        act.wait_ge(lg_read, NG * L + g + 1)
                        act.activation(ex[:, :, :], lg[:, :, :], ACT.Exp).then_inc(exp_done, 1)
                        for c, w in enumerate(FW):
                            n = 3 * g + c
                            k = (3 * gb + c) % 2
                            act.wait_ge(gu_done, 3 * NG * L + n + 1)
                            act.wait_ge(h_free, 3 * NG * L + n + 1)
                            act.activation(sg[0:w, k, :], bank[2 + 2 * k][0:w, :], ACT.Silu).then_inc(sg_ready, 1)
                        act.wait_ge(pos_done, NG * L + g + 1)
                        act.activation(pos[:, bass.ds(g * G, G), :], PO, ACT.Copy).then_inc(pos_saved, 1)

                def transposed(j, s):
                    act.wait_ge(xgt_done, j + 1 + (NB + 2) * L)
                    act.activation(xgt[:, s, :, :], bank[s][:, 0:D].rearrange("p (c t) -> p c t", c=DC),
                                   ACT.Copy).then_inc(xgt_ready, 1)

                def gated(j, s):
                    act.wait_ge(egu_done, j + 1 + (NB + 1) * L)
                    act.activation(sge[:, s, :], bank[2 + s][:, 0:F], ACT.Silu).then_inc(esg_ready, 1)

                transposed(0, 0)
                gated(0, 0)
                transposed(1, 1)
                with act.Fori(0, NB // U) as it:
                    for u in range(U):
                        j = it * U + u
                        act.wait_ge(eh_ready, j + (NB + 1) * L)
                        gated(j + 1, (u + 1) % 2)
                        transposed(j + 2, u % 2)

            def attention():
                act.wait_ge(stats, 2)
                act.activation(sd[:, :], mv[:, :, 1], ACT.Sqrt, bias=eps[:, 0:1]).then_inc(sd_ready, 1)
                with act.Fori(0, NG // 2) as it:
                    for gb in range(2):
                        g = it * 2 + gb
                        copy_tiles(NT, gb, g)
                        for c in range(2):
                            act.wait_ge(at_done, g * 4 + 2 * c + 1)
                            act.wait_ge(hid_ready, g * 2 + c)
                            act.activation(gates[:, c, :], bank[2 + 2 * c][:, :], ACT.Sigmoid,
                                           bias=bat[:, c:c + 1]).then_inc(at_act, 1)
                            act.wait_ge(at_done, g * 4 + 2 * c + 2)
                            act.activation(values[:, c, :], bank[3 + 2 * c][:, :], ACT.Tanh,
                                           bias=bat[:, 2 + c:3 + c]).then_inc(at_act, 1)

            moe(0)
            attention()
            moe(1)

        @block.vector
        def _(dve):
            step = Steps(dve, dve_step)
            for s in (h_free, eo_ready, at_x):
                dve.sem_inc(s, 2)
            dve.wait_ge(made, 14)

            def statistics(L, phase):
                n = {"moe0": 0, "attn": 1, "moe1": 2}[phase]
                with dve.Fori(0, NT // U) as q:
                    step.enter(q, 2 * U + 2)
                    for u in range(U):
                        step.mark(dve.bn_stats(st[:, u, :], xs[:, bass.ds(q * U + u, 1), :].rearrange("p a d -> p (a d)")))
                    step.sync()
                    step.mark_none()
                    for u in range(U):
                        step.mark(dve.bn_aggr(mv8[:, u, :], st[:, u, :]))
                    step.sync()
                    step.mark(dve.tensor_copy(mv[:, bass.ds(q * U, U), :], mv8[:, :, :]))
                    step.sync()
                step.leave(NT // U)
                dve.sem_inc(stats, 1)
                dve.wait_ge(sd_ready, n + 1)
                dve.reciprocal(rs[:, :], sd[:, :]).then_inc(rs_ready, 1)
                dve.wait_ge(rs_ready, n + 1)

            def normalise(first, g, store):
                dve.wait_ge(tx_done, first + g * G)
                for u in range(G):
                    if store is not None:
                        dve.wait_ge(xn_stored[u], 16 * (NG * store + g))
                    i = g * G + u
                    dve.tensor_scalar(xnb[:, u, :], xs[:, bass.ds(i, 1), :].rearrange("p a d -> p (a d)"),
                                      mv[:, bass.ds(i, 1), 0:1].rearrange("p a b -> p (a b)"), rs[:, bass.ds(i, 1)],
                                      ALU.subtract, ALU.mult).then_inc(xn_ready, 1)

            def softmax_top(L, g, gb):
                dve.wait_ge(lg_done, NG * L + g + 1)
                step.mark(dve.tensor_reduce(g4[:, 0, :], LG, X, ALU.max))
                step.sync()
                dve.tensor_tensor(lg[:, :, :], LG, g4[:, 0, :][:, :, None].broadcast_to([P, G, E]),
                                  ALU.subtract).then_inc(lg_read, 1)
                dve.wait_ge(exp_done, NG * L + g + 1)
                step.mark(dve.tensor_reduce(g4[:, 1, :], ex[:, :, :], X, ALU.add))
                step.sync()
                step.mark(dve.reciprocal(g4[:, 2, :], g4[:, 1, :]))
                step.sync()
                step.mark(dve.tensor_tensor(pr[:, :, :], ex[:, :, :], g4[:, 2, :][:, :, None].broadcast_to([P, G, E]), ALU.mult))
                step.sync()
                step.mark_none()
                for u in range(G):
                    step.mark(dve.max(top8[:, u, :], pr[:, u, :]))
                step.sync()
                step.mark_none()
                for u in range(G):
                    step.mark(dve.max_index(idx8[:, u, :], top8[:, u, :], pr[:, u, :]))
                step.mark(dve.tensor_copy(topp[:, bass.ds(g * G, G), :], top8[:, :, :]))
                step.sync()
                step.mark(dve.tensor_copy(idxf[:, :, :], idx8[:, :, :]))
                step.sync()
                hot = onehot[:, bass.ds(g * G, G), :, :]
                step.mark(dve.tensor_tensor(hot, iota[:, 0:E][:, None, None, :].broadcast_to([P, G, TOPK, E]),
                                            idxf[:, :, 0:TOPK][:, :, :, None].broadcast_to([P, G, TOPK, E]), ALU.is_equal))
                step.sync()
                dve.wait_ge(pos_done, NG * L + g)
                step.mark_none()
                with nc.allow_low_precision("counts up to 32 are exact"):
                    dve.tensor_reduce(mask[:, gb, :, :], onehot[:, bass.ds(g * G, G), :, :].rearrange("p t k e -> p t e k"), X,
                                      ALU.add).then_inc(mask_ready, 1)
                    dve.wait_ge(mask_ready, NG * L + g + 1)
                    step.mark(dve.tensor_reduce(msum[:, :], mask[:, gb, :, :].rearrange("p t e -> p e t"), X, ALU.add))
                step.sync()
                dve.wait_ge(carry_ready, (NG + 1) * L + g + 1)
                dve.tensor_tensor(carry[:, 1 - gb, :], carry[:, gb, :], msum[:, :], ALU.add).then_inc(carry_ready, 1)

            def plan(L):
                dve.wait_ge(cnt_done, L + 1)
                step.mark(dve.tensor_scalar(coli[0:E, 0:1], bank[0][0:E, 0:1], float(CAP), float(P - 1), ALU.min, ALU.add))
                step.sync()
                step.mark(dve.tensor_scalar(coli[0:E, 1:2], coli[0:E, 0:1], 7, None, ALU.arith_shift_right))
                step.sync()
                step.mark(dve.tensor_copy(nbf[:, :], coli[0:E, 1:2]))
                step.sync()
                dve.tensor_copy(nbb[:, :], nbf[:, 0:1].broadcast_to([E, P])).then_inc(nb_ready, 1)
                dve.wait_ge(start_done, L + 1)
                step.mark(dve.tensor_scalar(start[:, :], bank[1][:, 0:E], float(P), None, ALU.mult))
                step.mark(dve.tensor_copy(endrow[0:1, WR:WR + E], bank[1][0:1, E:2 * E]))
                step.mark(dve.tensor_copy(col[0:E, 0:1], bank[0][0:E, 8:9]))
                step.sync()
                dve.tensor_scalar(ge[:, :], iota[0:E, :], col[0:E, 0:1], None, ALU.is_ge).then_inc(ge_ready, 1)
                dve.wait_ge(e_done, L + 1)
                step.mark(dve.tensor_scalar(erow[0:1, 0:NB], bank[2][0:1, 0:NB], float(E - 1), None, ALU.min))
                step.sync()
                dve.sem_inc(plan_ready, 1)
                dve.wait_ge(pos_saved, NG * (L + 1))
                with dve.Fori(0, NG) as g:
                    step.enter(g, 6)
                    step.mark(dve.tensor_scalar(v1[:, :, :], pos[:, bass.ds(g * G, G), :], float(CAP), DROPPED, ALU.is_ge, ALU.mult))
                    step.mark(dve.tensor_tensor(v2[:, :, :], pos[:, bass.ds(g * G, G), :], start[:, :][:, None, :].broadcast_to([P, G, E]), ALU.add))
                    step.sync()
                    step.mark(dve.tensor_tensor(v3[:, :, :], v1[:, :, :], v2[:, :, :], ALU.add))
                    step.sync()
                    step.mark(dve.tensor_tensor(pick[:, :, :, :], onehot[:, bass.ds(g * G, G), :, :],
                                                v3[:, :, :][:, :, None, :].broadcast_to([P, G, TOPK, E]), ALU.mult))
                    step.sync()
                    step.mark_none()
                    step.mark(dve.tensor_reduce(slot[:, bass.ds(g * (G * TOPK), G * TOPK)].rearrange("p (t k) -> p t k", t=G), pick[:, :, :, :], X, ALU.add))
                    step.sync()
                step.leave(NG)
                step.mark(dve.tensor_copy(sloti[:, :], slot[:, :]))
                step.mark(dve.tensor_reduce(wsum[:, :], topp[:, :, 0:TOPK], X, ALU.add))
                step.mark(dve.tensor_scalar(wc[:, :, :], slot[:, :].rearrange("p (t k) -> p t k", t=NT), DROPPED, 0.5, ALU.is_lt, ALU.mult))
                step.sync()
                step.mark(dve.tensor_scalar(blki[:, :], sloti[:, :], 7, None, ALU.arith_shift_right))
                step.mark(dve.tensor_scalar(sloti[:, :], sloti[:, :], P - 1, None, ALU.bitwise_and))
                step.mark(dve.tensor_scalar(wsum[:, :], wsum[:, :], 1e-20, None, ALU.add))
                step.sync()
                step.mark(dve.tensor_copy(blk[:, :], blki[:, :]))
                step.mark(dve.tensor_copy(low[:, :], sloti[:, :]))
                step.mark(dve.reciprocal(wrec[:, :], wsum[:, :]))
                step.sync()
                step.mark(dve.tensor_tensor(wv[:, :, :], topp[:, :, 0:TOPK], wrec[:, :][:, :, None].broadcast_to([P, NT, TOPK]), ALU.mult))
                step.sync()
                step.mark(dve.tensor_tensor(wc[:, :, :], wv[:, :, :], wc[:, :, :], ALU.mult))
                with dve.Fori(0, NT // 2) as it:
                    step.enter(it, 2 * 3)
                    for s in range(2):
                        i = it * 2 + s
                        if s == 0:
                            dve.wait_ge(oh_used, NT * L + i)
                        step.mark(dve.tensor_copy(cur[:, s, 0, 0:TOPK], blk[:, bass.ds(i * TOPK, TOPK)]))
                        step.mark(dve.tensor_copy(cur[:, s, 1, 0:TOPK], low[:, bass.ds(i * TOPK, TOPK)]))
                        step.mark(dve.tensor_copy(cur[:, s, 0, 6:7], tokval[:, bass.ds(i, 1)]))
                    step.sync()
                    for s in range(2):
                        i = it * 2 + s
                        for k in range(TOPK):
                            dve.tensor_scalar(otok[:, s, k, :], iota[:, 0:P], cur[:, s, 1, k:k + 1], cur[:, s, 0, 6:7], ALU.is_equal, ALU.mult)
                            dve.tensor_scalar(orow[:, s, k, :], iota[:, 0:P], cur[:, s, 1, k:k + 1], float(k + 1), ALU.is_equal, ALU.mult)
                            dve.tensor_scalar(oblk[:, s, k, :], iota[:, :], cur[:, s, 0, k:k + 1], None, ALU.is_equal).then_inc(oh_ready, 1)
                step.leave(NT // 2)
                dve.wait_ge(list_done, L + 1)
                step.mark(dve.tensor_scalar(tok[:, 0:NB], bank[2][:, 0:NB], 2048.0, None, ALU.add))
                step.mark(dve.tensor_scalar(f1[:, :], bank[2][:, 0:NB], 2048.0, float(TOPK), ALU.add, ALU.mult))
                step.mark(dve.tensor_scalar(f2[:, :], bank[3][:, 0:NB], 0.0, 100000.0, ALU.is_equal, ALU.mult))
                step.sync()
                step.mark(dve.tensor_tensor(f1[:, :], f1[:, :], f2[:, :], ALU.add))
                step.sync()
                step.mark(dve.scalar_tensor_tensor(row[:, :], f1[:, :], -1.0, bank[3][:, 0:NB], ALU.add, ALU.add))
                step.sync()
                dve.sem_inc(list_ready, 1)

            def experts(L):
                eb, hb = NB * L, (NB + 1) * L

                def hidden(j, s):
                    dve.wait_ge(esg_ready, j + 1 + hb)
                    dve.tensor_tensor(he[:, s, :], sge[:, s, :], bank[2 + s][:, F:2 * F], ALU.mult).then_inc(eh_ready, 1)

                hidden(0, 0)
                with dve.Fori(0, NB // U) as it:
                    for u in range(U):
                        j = it * U + u
                        s = u % 2
                        dve.wait_ge(eht_done, j + 1 + eb)
                        dve.tensor_copy(het[0:FH, s, :, :], bank[4 + s][0:FH, 0:2 * P].rearrange("p (c t) -> p c t", c=2)).then_inc(eht_ready, 1)
                        hidden(j + 1, 1 - s)
                        dve.wait_ge(edn_done, j + 1 + eb)
                        dve.wait_ge(eo_out[u % 4], 16 * (it * 2 + u // 4 + NB // 4 * L))
                        dve.tensor_copy(eo[:, u % 4, :], bank[6 + s][:, 0:D]).then_inc(eo_ready, 1)

            def combine(L):
                with dve.Fori(0, NG) as g:
                    step.enter(g, G * (TOPK - 1))
                    for k in range(TOPK):
                        for u in range(G):
                            i = g * G + u
                            if k == 0:
                                dve.wait_ge(y_in[u], 16 * (NG * L + g + 1))
                            xi = xs[:, bass.ds(i, 1), :].rearrange("p a d -> p (a d)")
                            ins = dve.scalar_tensor_tensor(xi, yb[:, u, k * D:(k + 1) * D],
                                                           wc[:, bass.ds(i, 1), k:k + 1].rearrange("p a b -> p (a b)"), xi, ALU.mult, ALU.add)
                            if k < TOPK - 1:
                                step.mark(ins)
                            elif u == G - 1:
                                ins.then_inc(comb, 1)
                        if k < TOPK - 1:
                            step.sync()
                        else:
                            dve.wait_ge(comb, NG * L + g + 1)
                step.leave(NG)

            def moe(L):
                if L == 0:
                    for q in range(4):
                        dve.wait_ge(x_in_s[q], 16)
                statistics(L, f"moe{L}")
                step.mark(dve.memset(carry[:, 0, :], 0.0))
                step.sync()
                dve.sem_inc(carry_ready, 1)
                with dve.Fori(0, NG // 2) as it:
                    step.enter(it, 2 * 19)
                    for gb in range(2):
                        g = it * 2 + gb
                        normalise(tiles_before(f"moe{L}"), g, L)
                        softmax_top(L, g, gb)
                        for c, w in enumerate(FW):
                            n = 3 * g + c
                            k = (3 * gb + c) % 2
                            if c == 0:
                                dve.wait_ge(dn_done, NT * L + g * G)
                            dve.wait_ge(sg_ready, 3 * NG * L + n + 1)
                            dve.tensor_tensor(hs[0:w, c, :], sg[0:w, k, :], bank[3 + 2 * k][0:w, :], ALU.mult).then_inc(h_free, 1)
                        for u in range(G):
                            i = g * G + u
                            dve.wait_ge(dn_done, NT * L + i + 1)
                            xi = xs[:, bass.ds(i, 1), :].rearrange("p a d -> p (a d)")
                            dve.scalar_tensor_tensor(xi, bank[2 + u][:, 0:D], 0.5, xi, ALU.mult, ALU.add).then_inc(xs_added, 1)
                step.leave(NG // 2)
                plan(L)
                experts(L)
                dve.wait_ge(xs_added, NT * (L + 1))
                combine(L)

            def attention():
                statistics(0, "attn")
                for b in range(2):
                    step.mark(dve.memset(hid[:, 1, :, T - 1:T], 0.0))
                    step.sync()
                    with dve.Fori(0, NG // 4) as it:
                        for gb in range(2):
                            g = b * (NG // 2) + it * 2 + gb
                            normalise(NT, g, None)
                            dve.wait_ge(hid_ready, g * 2)
                            for c in range(2):
                                dve.wait_ge(at_act, g * 4 + 2 * c + 2)
                                dve.tensor_tensor_scan(hid[:, gb, c, :], gates[:, c, :], values[:, c, :],
                                                       hid[:, 1 - gb, c, T - 1:T], ALU.mult, ALU.add).then_inc(hid_ready, 1)
                            for u in range(G):
                                i = g * G + u
                                dve.wait_ge(ht_done, i + 1)
                                xi = xs[:, bass.ds(i, 1), :].rearrange("p a d -> p (a d)")
                                dve.tensor_tensor(xi, bank[6 + u % 2][:, 0:D], xi, ALU.add).then_inc(at_x, 1)
                dve.wait_ge(at_x, NT + 2)

            moe(0)
            attention()
            moe(1)

        @block.tensor
        def _(pe):
            pe.wait_ge(made, 14)
            pe.wait_ge(w_in, 16 * 8)

            def transpose_tile(first, g, u):
                pe.wait_ge(xn_ready, first + g * G + u + 1)
                pe.wait_ge(xt_free, first + g * G + u + 1)
                for c in range(DC):
                    last = pe.transpose(psT[u % 2][:, c * P:(c + 1) * P], xnb[:, u, c * P:(c + 1) * P], ident[:, :])
                last.then_inc(tx_done, 1)

            def route(L, g, gb):
                first = tiles_before(f"moe{L}")

                def logits(u):
                    pe.wait_ge(xt_free, first + g * G + u + 3)
                    for c in range(DC):
                        last = pe.matmul(LG[:, u, :], xt[:, gb, c, u * P:(u + 1) * P], gw[:, c, :], start=c == 0, stop=c == DC - 1)
                    if u == G - 1:
                        last.then_inc(lg_done, 1)

                for u in range(G):
                    transpose_tile(first, g, u)
                    if u == 0:
                        pe.wait_ge(pos_saved, NG * L + g)
                    if u:
                        logits(u - 1)
                logits(G - 1)

            def shared(L, g, gb):
                pe.wait_ge(xs_added, NT * L + g * G)
                for c, w in enumerate(FW):
                    n = 3 * g + c
                    k = (3 * gb + c) % 2
                    pe.wait_ge(h_free, 3 * NG * L + n + 1)
                    for wt, b in ((shg, bank[2 + 2 * k]), (shu, bank[3 + 2 * k])):
                        for d in range(DC):
                            last = pe.matmul(b[0:w, :], wt[:, d, FO[c]:FO[c] + w], xt[:, gb, d, :], start=d == 0, stop=d == DC - 1)
                    last.then_inc(gu_done, 1)

            def ranks(L, g, gb):
                pe.wait_ge(mask_ready, NG * L + g + 1)
                pe.wait_ge(carry_ready, (NG + 1) * L + g + 1)
                pe.matmul(PO, before[:, :], mask[:, gb, :, :], start=True, stop=False)
                for v in range(G - 1):
                    pe.matmul(PO[:, v + 1:G, :], ones[:, :], mask[:, gb, v, :][:, None, :].broadcast_to([P, G - 1 - v, E]),
                              start=False, stop=False, skip_group_check=True)
                pe.matmul(PO, ones[:, :], carry[:, gb, :][:, None, :].broadcast_to([P, G, E]), start=False, stop=True).then_inc(pos_done, 1)

            def shared_down(L, g):
                pe.wait_ge(h_free, 3 * NG * L + 3 * g + 3 + 2)
                for u in range(G):
                    for c, w in enumerate(FW):
                        last = pe.matmul(bank[2 + u][:, 0:D], hs[0:w, c, u * P:(u + 1) * P], shd[0:w, c, :], start=c == 0, stop=c == len(FW) - 1)
                    last.then_inc(dn_done, 1)

            def plan(L):
                pe.wait_ge(carry_ready, (NG + 1) * (L + 1))
                pe.wait_ge(pos_saved, NG * (L + 1))
                pe.matmul(bank[0][0:E, 0:1], carry[:, 0, :], ones[:, 0:1], start=True, stop=True).then_inc(cnt_done, 1)
                pe.wait_ge(nb_ready, L + 1)
                pe.matmul(bank[1][:, 0:E], nbb[:, :], before[0:E, 0:E], start=True, stop=True)
                pe.matmul(bank[1][:, E:2 * E], nbb[:, :], upto[0:E, 0:E], start=True, stop=True)
                pe.matmul(bank[0][0:E, 8:9], upto[0:E, 0:E], nbf[:, :], start=True, stop=True).then_inc(start_done, 1)
                pe.wait_ge(ge_ready, L + 1)
                pe.matmul(bank[2][:, 0:NB], ones[0:E, :], ge[:, :], start=True, stop=True).then_inc(e_done, 1)
                pe.wait_ge(plan_ready, L + 1)
                for b in (2, 3):
                    pe.matmul(bank[b][:, 0:NB], none[:, :], iota[:, :], start=True, stop=False)
                with pe.Fori(0, NT // 2) as it:
                    for s in range(2):
                        for k in range(TOPK):
                            pe.wait_ge(oh_ready, (it * 2 + s) * TOPK + k + 1 + NT * TOPK * L)
                            pe.matmul(bank[2][:, 0:NB], otok[:, s, k, :], oblk[:, s, k, :], start=False, stop=False, skip_group_check=True)
                            last = pe.matmul(bank[3][:, 0:NB], orow[:, s, k, :], oblk[:, s, k, :], start=False, stop=False, skip_group_check=True)
                        last.then_inc(oh_used, 1)
                for b in (2, 3):
                    last = pe.matmul(bank[b][:, 0:NB], none[:, :], iota[:, :], start=False, stop=True)
                last.then_inc(list_done, 1)

            def experts(L):
                def transposes(j, s8, turn, s):
                    pe.wait_ge(xg_in[s8], 16 * (turn + 1 + (NB // U + (s8 < AHEAD)) * L))
                    for c in range(DC):
                        last = pe.transpose(bank[s][:, c * P:(c + 1) * P], xg[:, s8, c * P:(c + 1) * P], ident[:, :])
                    last.then_inc(xgt_done, 1)

                def gate_up(j, s):
                    e = pe.value_load(erow[0:1, bass.ds(j, 1)], min_val=0, max_val=E - 1)
                    pe.wait_ge(w_ready, e + 1 + E * L)
                    pe.wait_ge(xgt_ready, j + 1 + (NB + 2) * L)
                    r = e % WR
                    for c in range(DC):
                        last = pe.matmul(bank[2 + s][:, 0:2 * F], xgt[:, s, c, :],
                                         wring[:, bass.ds(r, 1), c * 2 * F:(c + 1) * 2 * F].rearrange("p a m -> p (a m)"),
                                         start=c == 0, stop=c == DC - 1)
                    last.then_inc(egu_done, 1)

                def hidden_transposes(j, s):
                    pe.wait_ge(eh_ready, j + 1 + (NB + 1) * L)
                    for c in range(2):
                        last = pe.transpose(bank[4 + s][0:FH, c * P:(c + 1) * P], he[:, s, c * FH:(c + 1) * FH], ident[:, :])
                    last.then_inc(eht_done, 1)

                def down(j, s):
                    e = pe.value_load(erow[0:1, bass.ds(j, 1)], min_val=0, max_val=E - 1)
                    r = e % WR
                    pe.wait_ge(eht_ready, j + 1 + NB * L)
                    pe.wait_ge(eo_ready, j + 1 + NB * L)
                    for c in range(2):
                        last = pe.matmul(bank[6 + s][:, 0:D], het[0:FH, s, c, :],
                                         wring[0:FH, bass.ds(r, 1), WG + c * D:WG + (c + 1) * D].rearrange("p a m -> p (a m)"),
                                         start=c == 0, stop=c == 1)
                    last.then_inc(edn_done, 1)

                transposes(0, 0, 0, 0)
                gate_up(0, 0)
                transposes(1, 1, 0, 1)
                with pe.Fori(0, NB // U) as it:
                    for u in range(U):
                        j = it * U + u
                        hidden_transposes(j, u % 2)
                        gate_up(j + 1, (u + 1) % 2)
                        down(j, u % 2)
                        transposes(j + 2, (u + 2) % U, it + (u + 2) // U, u % 2)

            def moe(L):
                with pe.Fori(0, NG // 2) as it:
                    for gb in range(2):
                        g = it * 2 + gb
                        route(L, g, gb)
                        shared(L, g, gb)
                        ranks(L, g, gb)
                        shared_down(L, g)
                plan(L)
                experts(L)

            def attention():
                with pe.Fori(0, NG // 2) as it:
                    for gb in range(2):
                        g = it * 2 + gb
                        for u in range(G):
                            transpose_tile(NT, g, u)
                        pe.wait_ge(xt_free, NT + g * G + G + 2)
                        for c in range(2):
                            for v in range(2):
                                pe.wait_ge(at_act, g * 4)
                                for d in range(DC):
                                    m = (2 * v + c) * P
                                    last = pe.matmul(bank[2 + 2 * c + v][:, :], wat[:, d, m:m + P], xt[:, gb, d, :], start=d == 0, stop=d == DC - 1)
                                last.then_inc(at_done, 1)
                        pe.wait_ge(hid_ready, g * 2 + 2)
                        for u in range(G):
                            i = g * G + u
                            pe.wait_ge(at_x, i + 1)
                            for c in range(2):
                                last = pe.transpose(bank[6 + u % 2][:, c * P:(c + 1) * P], hid[:, gb, c, u * P:(u + 1) * P], ident[:, :])
                            last.then_inc(ht_done, 1)

            moe(0)
            attention()
            moe(1)


def kernel(**inputs):
    import numpy as np
    import concourse.bacc as bacc
    from concourse.bass_utils import run_bass_kernel_spmd

    x = np.asarray(inputs["L0_attn_x"])
    B, S, D = x.shape
    TOPK, CAP_FACTOR = 6, 2

    def chunked(wt):
        return np.ascontiguousarray(wt.reshape(D // 128, 128, -1).transpose(1, 0, 2))

    wg, wu, wd = (np.asarray(inputs[f"L0_ffn_w_{n}"]) for n in ("gate", "up", "down"))
    E, F, _ = wg.shape
    CAP = CAP_FACTOR * ((B * S * TOPK + E - 1) // E)
    gu = np.concatenate([wg, wu], axis=1).transpose(0, 2, 1)
    gu = gu.reshape(E, D // 128, 128, 2 * F).transpose(0, 2, 1, 3).reshape(E, 128, -1)
    dn = wd.transpose(0, 2, 1).reshape(E, 2, F // 2, D).transpose(0, 2, 1, 3).reshape(E, F // 2, -1)
    arrays = {
        "x_rows": x.reshape(B * S, D),
        "w_attn": chunked(np.asarray(inputs["L0_attn_W"]).T),
        "b_attn": np.ascontiguousarray(np.asarray(inputs["L0_attn_b"]).reshape(-1, 128).T),
        "gate_w": chunked(np.asarray(inputs["L0_ffn_gate_w"]).T),
        "w_gate_up": np.ascontiguousarray(gu),
        "w_down": np.ascontiguousarray(dn),
        "sh_gate": chunked(np.asarray(inputs["L0_ffn_sh_gate"]).T),
        "sh_up": chunked(np.asarray(inputs["L0_ffn_sh_up"]).T),
        "sh_down": np.ascontiguousarray(np.asarray(inputs["L0_ffn_sh_down"]).T),
    }
    nc = bacc.Bacc("TRN2", target_bir_lowering=False, num_devices=1)
    args = [nc.dram_tensor(n, a.shape, F32, kind="ExternalInput").ap() for n, a in arrays.items()]
    out = nc.dram_tensor("out_rows", (B * S, D), F32, kind="ExternalOutput").ap()
    macaron(nc, *args, out, TOPK, CAP)
    r = run_bass_kernel_spmd(nc, [arrays], core_ids=[0])
    return r.results[0]["out_rows"].reshape(B, S, D)
```
